# Optimizing a Trainium2 kernel written in Bass

```python
import numpy as np
import jax
import jax.numpy as jnp

def _softmax(x, axis=-1):
    return jax.nn.softmax(x, axis=axis)

def _gelu(x):
    return jax.nn.gelu(x, approximate=True)

def _silu(x):
    return jax.nn.silu(x)

def _sigmoid(x):
    return jax.nn.sigmoid(x)

def _layernorm(x, axis=-1, eps=1e-05):
    m = jnp.mean(x, axis=axis, keepdims=True)
    v = jnp.var(x, axis=axis, keepdims=True)
    return (x - m) / jnp.sqrt(v + eps)

def _scatter_add(tgt, idx, src, axis=0):
    return tgt.at[idx].add(src)

def _segment_sum(src, seg, n):
    return jax.ops.segment_sum(src, seg, n)
kernel_name = 'mk_cond_resid_d2_seqx_r4_fa9c6d'

def setup_inputs(seed: int=0):
    np.random.seed(seed)
    _w = jnp.asarray

    def _rec_inputs():
        import jax
        import jax.numpy as jnp
        _rk = jax.random.key(seed)
        x = -7.109e-05 + 0.9999 * jax.random.normal(jax.random.fold_in(_rk, 1), (8, 256, 1024), jnp.float32)
        _lenS = 256 - jax.random.randint(jax.random.fold_in(_rk, 7), (8,), 0, max(1, 256 // 4) + 1, jnp.int32)
        _lenS2 = 256 - jax.random.randint(jax.random.fold_in(_rk, 8), (8,), 0, max(1, 256 // 4) + 1, jnp.int32)
        itok_B_1_14 = jax.random.randint(jax.random.fold_in(_rk, 11), (8,), 1, 15, jnp.int32)
        itok_B_3_7 = jax.random.randint(jax.random.fold_in(_rk, 12), (8,), 3, 8, jnp.int32)
        return (x, itok_B_1_14, itok_B_3_7)
    x, itok_B_1_14, itok_B_3_7 = _rec_inputs()

    def _L0_cond_setup():
        import jax, jax.numpy as jnp
        import numpy as np
        B, S, D_IN = (8, 512, 1024)
        A, D_OUT = (16, 1024)
        key = jax.random.key(seed)
        k1, k2, k3 = jax.random.split(key, 3)
        x = jax.random.normal(k1, (B, S, D_IN), dtype=jnp.float32)
        weight = jax.random.normal(k2, (A, D_OUT, D_IN), dtype=jnp.float32) * 0.02
        adapter_ids = jax.random.randint(k3, (B,), 0, A, dtype=jnp.int64)
        return {'x': x, 'weight': weight, 'adapter_ids': adapter_ids}
    _L0_cond_all = _L0_cond_setup()
    _L0_cond_in = {k: v for k, v in _L0_cond_all.items() if k in ('weight',)}
    del _L0_cond_all

    def _L1_cond_setup():
        import jax, jax.numpy as jnp
        import numpy as np
        MAX_LORAS, OUT, IN = (8, 1024, 1024)
        B, S = (4, 512)
        key = jax.random.key(seed)
        k1, k2, k3 = jax.random.split(key, 3)
        x = jax.random.normal(k1, (B, S, IN), dtype=jnp.float32)
        weight = jax.random.normal(k2, (MAX_LORAS, OUT, IN), dtype=jnp.float32) * 0.02
        adapter_ids = jax.random.randint(k3, (B,), 0, MAX_LORAS, dtype=jnp.int32)
        return {'x': x, 'weight': weight, 'adapter_ids': adapter_ids}
    _L1_cond_all = _L1_cond_setup()
    _L1_cond_in = {k: v for k, v in _L1_cond_all.items() if k in ('weight',)}
    del _L1_cond_all
    return {'x': x, 'itok_B_1_14': itok_B_1_14, 'itok_B_3_7': itok_B_3_7, 'L0_cond_weight': _L0_cond_in['weight'], 'L1_cond_weight': _L1_cond_in['weight']}

def reference(x, itok_B_1_14, itok_B_3_7, L0_cond_weight, L1_cond_weight):
    import jax
    import jax.numpy as jnp

    def _L0_cond_ref(x, weight, adapter_ids):
        import jax, jax.numpy as jnp
        import numpy as np
        B, S, D_IN = (8, 512, 1024)
        A, D_OUT = (16, 1024)
        w = weight[adapter_ids]
        return jnp.einsum('bij,bkj->bik', x, w)

    def _L1_cond_ref(x, weight, adapter_ids):
        import jax, jax.numpy as jnp
        import numpy as np
        MAX_LORAS, OUT, IN = (8, 1024, 1024)
        B, S = (4, 512)
        w = weight[adapter_ids]
        return jnp.einsum('bsi,boi->bso', x, w)
    x = x + _L0_cond_ref(x, L0_cond_weight, itok_B_1_14)
    x = x + _L1_cond_ref(x, L1_cond_weight, itok_B_3_7)
    return x

_drawn_inputs = setup_inputs


def setup_inputs(seed=0):
    import zlib

    import numpy as np

    out = dict(_drawn_inputs(seed))
    spreads = {}
    factors = {}
    for name, (base, spread) in spreads.items():
        noise = np.random.default_rng([zlib.crc32(name.encode()), seed]).standard_normal(out[name].shape)
        drawn = base * np.exp(spread * noise) if base else spread * noise
        out[name] = jnp.asarray(drawn.astype(out[name].dtype))
    for name, factor in factors.items():
        out[name] = (out[name] * factor).astype(out[name].dtype)
    return out
```

```python
from contextlib import ExitStack

import concourse.bass as bass
from concourse import mybir
from concourse.alu_op_type import AluOpType as ALU

F32 = mybir.dt.float32
F32R = mybir.dt.float32r
P = 128
QUADRANTS = 4
BLOCK = P // QUADRANTS
BANK = 512
RING = 4
LEAD = 3


def residual_adapters(nc, x, ids0, ids1, weights0, weights1, out):
    B, S, D = x.shape
    A0, A1 = weights0.shape[0], weights1.shape[0]
    ROWS = S // P
    TILES = D // P
    HALVES = D // BANK
    PAIRS = TILES // 2
    UNITS = HALVES * PAIRS
    WIDE = D // QUADRANTS
    LAST = 2 * B - 1
    ADDS = HALVES * ROWS
    COPIES = ROWS
    W_DMA = 16 * QUADRANTS
    assert ROWS == 2 and HALVES == 2 and PAIRS == RING and TILES * BLOCK == WIDE

    with ExitStack() as ctx:
        def sb(name, shape, dtype):
            return ctx.enter_context(nc.sbuf_tensor(name, shape, dtype))

        def sem(name):
            return ctx.enter_context(nc.semaphore(name))

        raw = [[sb(f"raw{s}{h}", [P, BANK // BLOCK, WIDE], F32) for h in range(HALVES)] for s in range(2)]
        turned = sb("turned", [P, RING, 2, BANK], F32)
        w_hi = sb("w_hi", [P, RING, 2, BANK], F32R)
        w_lo = sb("w_lo", [P, RING, 2, BANK], F32R)
        x_rows = sb("x_rows", [P, ROWS, D], F32)
        mid_rows = sb("mid_rows", [P, ROWS, D], F32)
        rows = [sb(f"rows{s}", [P, ROWS, D], F32) for s in range(2)]
        out_rows = sb("out_rows", [P, ROWS, D], F32)
        a_hi = [sb(f"a_hi{s}", [P, TILES, S], F32R) for s in range(2)]
        a_lo = [sb(f"a_lo{s}", [P, TILES, S], F32R) for s in range(2)]
        ident = sb("ident", [P, P], F32)
        acc = [[ctx.enter_context(nc.psum_tensor(f"acc{h}{i}", [P, BANK], F32)) for i in range(ROWS)]
               for h in range(HALVES)]
        turn = [ctx.enter_context(nc.psum_tensor(f"turn{g}", [P, 2, S], F32)) for g in range(PAIRS)]

        raw_landed = [[sem(f"raw_landed{s}{h}") for h in range(HALVES)] for s in range(2)]
        start_landed = sem("start_landed")
        x_landed = sem("x_landed")
        x1_landed = sem("x1_landed")
        zeroed = sem("zeroed")
        ident_ready = sem("ident_ready")
        w_turned = sem("w_turned")
        w_hi_ready = sem("w_hi_ready")
        w_lo_ready = sem("w_lo_ready")
        a_turned = sem("a_turned")
        a_hi_ready = sem("a_hi_ready")
        a_lo_ready = sem("a_lo_ready")
        rows_ready = sem("rows_ready")
        multiplied = sem("multiplied")
        added = sem("added")
        stored = [sem(f"stored{h}") for h in range(HALVES)]

        block = ctx.enter_context(nc.Block())

        @block.sync
        def _(sp):
            def load_weights(weights, adapter, parity, h, first=0, last=WIDE, landed=None):
                for q in range(QUADRANTS):
                    sp.dma_start(
                        raw[parity][h][BLOCK * q:BLOCK * (q + 1), :, first:last],
                        weights[adapter, BANK * h:BANK * (h + 1), WIDE * q + first:WIDE * q + last]
                        .rearrange("(b k) j -> k b j", k=BLOCK),
                    ).then_inc(landed or raw_landed[parity][h], 16)

            def adapter_of(ids, b, count):
                return sp.value_load(ids[0:1, bass.ds(b, 1)], min_val=0, max_val=count - 1)

            def next_weights(stage, parity, weights, adapter, h):
                sp.wait_ge(w_turned, UNITS * stage + PAIRS * (h + 1))
                load_weights(weights, adapter, parity, h)

            def store(b, stage, h):
                sp.wait_ge(added, ADDS * stage + ROWS * (h + 1))
                sp.dma_start(out[b, :, BANK * h:BANK * (h + 1)].rearrange("(i p) k -> p i k", p=P),
                             out_rows[:, :, BANK * h:BANK * (h + 1)]).then_inc(stored[h], 16)

            adapter = adapter_of(ids0, 0, A0)
            load_weights(weights0, adapter, 0, 0, 0, WIDE // 2, start_landed)
            load_weights(weights0, adapter, 0, 0, WIDE // 2, WIDE)
            load_weights(weights0, adapter, 0, 1)
            sp.dma_start(mid_rows[:, :, :], x[1].rearrange("(i p) j -> p i j", p=P)).then_inc(x1_landed, 16)
            adapter = adapter_of(ids0, 1, A0)
            load_weights(weights0, adapter, 1, 0)
            load_weights(weights0, adapter, 1, 1)
            adapter = adapter_of(ids1, 0, A1)
            next_weights(0, 0, weights1, adapter, 0)
            next_weights(0, 0, weights1, adapter, 1)
            with sp.Fori(0, B - 2) as b:
                sp.wait_ge(rows_ready, COPIES * (2 * b + 2))
                sp.dma_start(x_rows[:, :, :], x[b + 2].rearrange("(i p) j -> p i j", p=P)).then_inc(x_landed, 16)
                adapter = adapter_of(ids0, b + 2, A0)
                next_weights(2 * b + 1, 1, weights0, adapter, 0)
                next_weights(2 * b + 1, 1, weights0, adapter, 1)
                adapter = adapter_of(ids1, b + 1, A1)
                next_weights(2 * b + 2, 0, weights1, adapter, 0)
                store(b, 2 * b + 2, 0)
                next_weights(2 * b + 2, 0, weights1, adapter, 1)
                store(b, 2 * b + 2, 1)
            adapter = adapter_of(ids1, B - 1, A1)
            next_weights(LAST - 2, 1, weights1, adapter, 0)
            next_weights(LAST - 2, 1, weights1, adapter, 1)
            for h in range(HALVES):
                store(B - 2, LAST - 1, h)
            for h in range(HALVES):
                store(B - 1, LAST, h)
            for h in range(HALVES):
                sp.wait_ge(stored[h], 16 * B)

        @block.vector
        def _(dve):
            def turn_weights(stage, parity, u):
                h, pair = u // PAIRS, u % PAIRS
                if isinstance(stage, int) and stage == 0:
                    if u == 0:
                        dve.wait_ge(start_landed, W_DMA)
                    if u in (PAIRS // 2, PAIRS):
                        dve.wait_ge(raw_landed[0][h], W_DMA)
                elif pair == 0:
                    dve.wait_ge(raw_landed[parity][h], (stage + 2 - parity) * (W_DMA // 2))
                if not (isinstance(stage, int) and stage == 0 and u < RING):
                    dve.wait_ge(w_lo_ready, UNITS * stage + u + 1 - RING)
                nc.vector.transpose(
                    turned[:, u % RING, :, :].rearrange("p t (b k) -> p t b k", k=BLOCK),
                    raw[parity][h][:, :, 2 * BLOCK * pair:2 * BLOCK * (pair + 1)]
                    .rearrange("p b (t r) -> p t b r", t=2),
                ).then_inc(w_turned, 1)

            def row_remainders(stage, parity, g):
                dve.wait_ge(a_hi_ready, PAIRS * stage + g + 1)
                nc.vector.tensor_tensor(a_lo[parity][:, 2 * g:2 * g + 2, :], turn[g][:, :, :],
                                        a_hi[parity][:, 2 * g:2 * g + 2, :].bitcast(F32),
                                        ALU.subtract).then_inc(a_lo_ready, 1)

            def add_rows(stage, parity, h, result, batch):
                if result is out_rows and not (isinstance(batch, int) and batch == 0):
                    dve.wait_ge(stored[h], 16 * batch)
                dve.wait_ge(multiplied, UNITS * stage + PAIRS * (h + 1))
                for i in range(ROWS):
                    quads = slice(QUADRANTS // HALVES * h, QUADRANTS // HALVES * (h + 1))
                    nc.vector.tensor_tensor(
                        result[:, i, :].rearrange("p (q t r) -> p q t r", q=QUADRANTS, r=BLOCK)[:, quads],
                        acc[h][i][:, :].rearrange("p (q t r) -> p q t r", t=TILES, r=BLOCK),
                        rows[parity][:, i, :].rearrange("p (t q r) -> p q t r", q=QUADRANTS, r=BLOCK)[:, quads],
                        ALU.add).then_inc(added, 1)

            def run_stage(stage, parity, result, before, last=False):
                for u in range(UNITS):
                    v = (u + LEAD) % UNITS
                    if u + LEAD < UNITS:
                        turn_weights(stage, parity, v)
                    elif not last:
                        turn_weights(stage + 1, 1 - parity, v)
                    if u == 0 and before:
                        add_rows(stage - 1, 1 - parity, 1, *before)
                    if u == PAIRS:
                        if result[0] is mid_rows:
                            dve.wait_ge(rows_ready, COPIES * (stage + 2))
                        add_rows(stage, parity, 0, *result)
                    if 1 <= u <= PAIRS and not last:
                        row_remainders(stage + 1, 1 - parity, u - 1)

            for g in range(PAIRS):
                row_remainders(0, 0, g)
            for u in range(LEAD):
                turn_weights(0, 0, u)
            run_stage(0, 0, (mid_rows, 0), None)
            run_stage(1, 1, (mid_rows, 1), (mid_rows, 0))
            run_stage(2, 0, (out_rows, 0), (mid_rows, 1))
            run_stage(3, 1, (mid_rows, 2), (out_rows, 0))
            with dve.Fori(1, B - 2) as b:
                run_stage(2 * b + 2, 0, (out_rows, b), (mid_rows, b + 1))
                run_stage(2 * b + 3, 1, (mid_rows, b + 2), (out_rows, b))
            run_stage(LAST - 1, 0, (out_rows, B - 2), (mid_rows, B - 1))
            run_stage(LAST, 1, (out_rows, B - 1), (out_rows, B - 2), last=True)
            add_rows(LAST, 1, 1, out_rows, B - 1)

        @block.scalar
        def _(act):
            def round_weights(stage, u):
                if not (isinstance(stage, int) and stage == 0 and u < RING):
                    act.wait_ge(multiplied, UNITS * stage + u + 1 - RING)
                act.wait_ge(w_turned, UNITS * stage + u + 1)
                nc.scalar.copy(w_hi[:, u % RING, :, :], turned[:, u % RING, :, :]).then_inc(w_hi_ready, 1)

            def round_rows(stage, parity, g):
                act.wait_ge(a_turned, PAIRS * stage + g + 1)
                nc.scalar.copy(a_hi[parity][:, 2 * g:2 * g + 2, :], turn[g][:, :, :]).then_inc(a_hi_ready, 1)

            def bring_rows(parity, source, i):
                nc.scalar.copy(rows[parity][:, i, :].rearrange("p (t q r) -> p t q r", q=QUADRANTS, r=BLOCK),
                               source[:, i, :].rearrange("p (q t r) -> p t q r", q=QUADRANTS, r=BLOCK)
                               ).then_inc(rows_ready, 1)

            def run_stage(stage, parity, source, landed, last=False):
                for u in range(UNITS):
                    if u + LEAD < UNITS:
                        round_weights(stage, u + LEAD)
                    elif not last:
                        round_weights(stage + 1, u + LEAD - UNITS)
                    if u == 0 and not last:
                        if landed:
                            act.wait_ge(*landed)
                        if not (isinstance(stage, int) and stage == 0):
                            act.wait_ge(added, ADDS * stage)
                    if u < ROWS and not last:
                        bring_rows(1 - parity, source, u)
                    if 1 <= u <= PAIRS and not last:
                        round_rows(stage + 1, 1 - parity, u - 1)

            act.dma_start(x_rows[:, :, :], x[0].rearrange("(i p) j -> p i j", p=P)).then_inc(x_landed, 16)
            act.wait_ge(x_landed, 16)
            for i in range(ROWS):
                bring_rows(0, x_rows, i)
            for g in range(PAIRS):
                round_rows(0, 0, g)
            for u in range(LEAD):
                round_weights(0, u)
            run_stage(0, 0, mid_rows, (x1_landed, 16))
            with act.Fori(0, B - 2) as b:
                run_stage(2 * b + 1, 1, mid_rows, None)
                run_stage(2 * b + 2, 0, x_rows, (x_landed, 16 * (b + 2)))
            run_stage(LAST - 2, 1, mid_rows, None)
            run_stage(LAST - 1, 0, mid_rows, None)
            run_stage(LAST, 1, None, None, last=True)

        @block.gpsimd
        def _(pool):
            nc.gpsimd.memset(ident[:, :], 0.0).then_inc(zeroed, 1)
            pool.wait_ge(zeroed, 1)
            nc.gpsimd.affine_select(out=ident[:, :], in_=ident[:, :], compare_op=ALU.not_equal, fill=1.0, base=0,
                                    pattern=[[-1, P]], channel_multiplier=1).then_inc(ident_ready, 1)
            with pool.Fori(0, (LAST + 1) * UNITS // RING) as turn_of_ring:
                for slot in range(RING):
                    pool.wait_ge(w_hi_ready, RING * turn_of_ring + slot + 1)
                    nc.gpsimd.tensor_tensor(w_lo[:, slot, :, :], turned[:, slot, :, :],
                                            w_hi[:, slot, :, :].bitcast(F32), ALU.subtract).then_inc(w_lo_ready, 1)

        @block.tensor
        def _(pe):
            def turn_rows(parity, g):
                for t in (2 * g, 2 * g + 1):
                    for i in range(ROWS):
                        done = pe.transpose(turn[g][:, t % 2, P * i:P * (i + 1)], rows[parity][:, i, P * t:P * (t + 1)],
                                            ident[:, :])
                done.then_inc(a_turned, 1)

            def multiply(stage, parity, u):
                h, pair = u // PAIRS, u % PAIRS
                if h == 0:
                    pe.wait_ge(a_lo_ready, PAIRS * stage + pair + 1)
                if pair == 0 and not (isinstance(stage, int) and stage == 0):
                    pe.wait_ge(added, ADDS * (stage - 1) + ROWS * (h + 1))
                pe.wait_ge(w_lo_ready, UNITS * stage + u + 1)
                for t in range(2):
                    for i in range(ROWS):
                        mine = slice(P * i, P * (i + 1))
                        tile = 2 * pair + t
                        hi, lo = a_hi[parity][:, tile, mine], a_lo[parity][:, tile, mine]
                        first, last = tile == 0, tile == TILES - 1
                        pe.matmul(acc[h][i][:, :], hi, w_hi[:, u % RING, t, :], start=first, stop=False)
                        pe.matmul(acc[h][i][:, :], hi, w_lo[:, u % RING, t, :], start=False, stop=False)
                        done = pe.matmul(acc[h][i][:, :], lo, w_hi[:, u % RING, t, :], start=False, stop=last)
                done.then_inc(multiplied, 1)

            def run_stage(stage, parity, last=False):
                for u in range(UNITS):
                    multiply(stage, parity, u)
                    if 1 <= u <= PAIRS and not last:
                        if u == 1:
                            pe.wait_ge(rows_ready, COPIES * (stage + 2))
                        turn_rows(1 - parity, u - 1)

            pe.wait_ge(ident_ready, 1)
            pe.wait_ge(rows_ready, COPIES)
            for g in range(PAIRS):
                turn_rows(0, g)
            run_stage(0, 0)
            with pe.Fori(0, B - 2) as b:
                run_stage(2 * b + 1, 1)
                run_stage(2 * b + 2, 0)
            run_stage(LAST - 2, 1)
            run_stage(LAST - 1, 0)
            run_stage(LAST, 1, last=True)


def kernel(x, itok_B_1_14, itok_B_3_7, L0_cond_weight, L1_cond_weight):
    import numpy as np
    import concourse.bacc as bacc
    from concourse.bass_utils import run_bass_kernel_spmd

    nc = bacc.Bacc("TRN2", target_bir_lowering=False, num_devices=1)
    arrays = {
        "x": np.ascontiguousarray(x),
        "ids0": np.ascontiguousarray(itok_B_1_14).reshape(1, -1),
        "ids1": np.ascontiguousarray(itok_B_3_7).reshape(1, -1),
        "weights0": np.ascontiguousarray(L0_cond_weight),
        "weights1": np.ascontiguousarray(L1_cond_weight),
    }
    ins = [nc.dram_tensor(n, a.shape, mybir.dt.from_np(a.dtype), kind="ExternalInput").ap()
           for n, a in arrays.items()]
    out = nc.dram_tensor("out", arrays["x"].shape, F32, kind="ExternalOutput").ap()
    residual_adapters(nc, *ins, out)
    return run_bass_kernel_spmd(nc, [arrays], core_ids=[0]).results[0]["out"]
```

```python
from contextlib import ExitStack

import concourse.bass as bass
from concourse import mybir
from concourse.alu_op_type import AluOpType as ALU

F32 = mybir.dt.float32
F32R = mybir.dt.float32r
P = 128
QUADRANTS = 4
BLOCK = P // QUADRANTS
BANK = 512
RING = 4
LEAD = 3
ROWS_AT = 4


def residual_adapters(nc, x, ids0, ids1, weights0, weights1, out):
    B, S, D = x.shape
    A0, A1 = weights0.shape[0], weights1.shape[0]
    ROWS = S // P
    TILES = D // P
    HALVES = D // BANK
    PAIRS = TILES // 2
    UNITS = HALVES * PAIRS
    WIDE = D // QUADRANTS
    LAST = 2 * B - 1
    ADDS = HALVES * ROWS
    IN_BLOCKS = 16 * QUADRANTS
    RELAID = 16 * QUADRANTS * QUADRANTS
    assert ROWS == 2 and HALVES == 2 and PAIRS == RING and TILES * BLOCK == WIDE and ROWS_AT + PAIRS == UNITS

    with ExitStack() as ctx:
        def sb(name, shape, dtype):
            return ctx.enter_context(nc.sbuf_tensor(name, shape, dtype))

        def sem(name):
            return ctx.enter_context(nc.semaphore(name))

        raw = [[sb(f"raw{s}{h}", [P, BANK // BLOCK, WIDE], F32) for h in range(HALVES)] for s in range(2)]
        blocks = [sb(f"blocks{s}", [P, S // BLOCK, WIDE], F32) for s in range(2)]
        kept = [sb(f"kept{s}", [P, ROWS, D], F32) for s in range(2)]
        a_hi = [sb(f"a_hi{s}", [P, TILES, S], F32R) for s in range(2)]
        a_lo = [sb(f"a_lo{s}", [P, TILES, S], F32R) for s in range(2)]
        turned = sb("turned", [P, RING, 2, BANK], F32)
        w_hi = sb("w_hi", [P, RING, 2, BANK], F32R)
        w_lo = sb("w_lo", [P, RING, 2, BANK], F32R)
        mid_rows = sb("mid_rows", [P, ROWS, D], F32)
        out_rows = sb("out_rows", [P, ROWS, D], F32)
        acc = [[ctx.enter_context(nc.psum_tensor(f"acc{h}{i}", [P, BANK], F32)) for i in range(ROWS)]
               for h in range(HALVES)]
        a_turned = [ctx.enter_context(nc.psum_tensor(f"a_turned{g}", [P, 2, S], F32)) for g in range(PAIRS)]

        raw_landed = [[sem(f"raw_landed{s}{h}") for h in range(HALVES)] for s in range(2)]
        start_landed = sem("start_landed")
        x0_blocks_landed = sem("x0_blocks_landed")
        x_blocks_landed = sem("x_blocks_landed")
        x0_landed = sem("x0_landed")
        x_landed = sem("x_landed")
        relaid = sem("relaid")
        mid_kept = sem("mid_kept")
        w_turned = sem("w_turned")
        w_hi_ready = sem("w_hi_ready")
        w_lo_ready = sem("w_lo_ready")
        rows_turned = sem("rows_turned")
        a_hi_ready = sem("a_hi_ready")
        a_lo_ready = sem("a_lo_ready")
        multiplied = sem("multiplied")
        first_rows_closed = sem("first_rows_closed")
        added = sem("added")
        stored = [sem(f"stored{h}") for h in range(HALVES)]

        block = ctx.enter_context(nc.Block())

        @block.sync
        def _(sp):
            def load_weights(weights, adapter, parity, h, first=0, last=WIDE, landed=None):
                for q in range(QUADRANTS):
                    sp.dma_start(
                        raw[parity][h][BLOCK * q:BLOCK * (q + 1), :, first:last],
                        weights[adapter, BANK * h:BANK * (h + 1), WIDE * q + first:WIDE * q + last]
                        .rearrange("(b k) j -> k b j", k=BLOCK),
                    ).then_inc(landed or raw_landed[parity][h], 16)

            def adapter_of(ids, b, count):
                return sp.value_load(ids[0:1, bass.ds(b, 1)], min_val=0, max_val=count - 1)

            def next_weights(stage, parity, weights, adapter, h):
                sp.wait_ge(w_turned, UNITS * stage + PAIRS * (h + 1))
                load_weights(weights, adapter, parity, h)

            def load_x(b, parity, landed, blocks_landed):
                for q in range(QUADRANTS):
                    sp.dma_start(blocks[parity][BLOCK * q:BLOCK * (q + 1), :, :],
                                 x[b, :, WIDE * q:WIDE * (q + 1)].rearrange("(c r) j -> r c j", r=BLOCK)
                                 ).then_inc(blocks_landed, 16)
                sp.dma_start(kept[parity][:, :, :], x[b].rearrange("(i p) j -> p i j", p=P)).then_inc(landed, 16)

            def relay(stage, h, parity):
                sp.wait_ge(added, ADDS * stage + ROWS * (h + 1))
                for q in range(QUADRANTS // HALVES * h, QUADRANTS // HALVES * (h + 1)):
                    for g in range(QUADRANTS):
                        sp.dma_start(blocks[parity][BLOCK * q:BLOCK * (q + 1), g:S // BLOCK:QUADRANTS, :],
                                     mid_rows[BLOCK * g:BLOCK * (g + 1), :, WIDE * q:WIDE * (q + 1)]
                                     ).then_inc(relaid, 16)

            def store(b, stage, h, tiles=slice(0, ROWS)):
                sp.wait_ge(added, ADDS * stage + ROWS * h + tiles.stop)
                cols = slice(BANK * h, BANK * (h + 1))
                sp.dma_start(out[b, :, cols].rearrange("(i p) k -> p i k", p=P)[:, tiles],
                             out_rows[:, tiles, cols]).then_inc(stored[h], 16)

            adapter = adapter_of(ids0, 0, A0)
            load_weights(weights0, adapter, 0, 0, 0, WIDE // 2, start_landed)
            load_weights(weights0, adapter, 0, 0, WIDE // 2, WIDE)
            load_weights(weights0, adapter, 0, 1)
            load_x(1, 1, x_landed, x_blocks_landed)
            adapter = adapter_of(ids0, 1, A0)
            load_weights(weights0, adapter, 1, 0)
            load_weights(weights0, adapter, 1, 1)
            adapter = adapter_of(ids1, 0, A1)
            next_weights(0, 0, weights1, adapter, 0)
            next_weights(0, 0, weights1, adapter, 1)
            relay(0, 0, 0)
            relay(0, 1, 0)
            with sp.Fori(0, B - 2) as b:
                adapter = adapter_of(ids0, b + 2, A0)
                next_weights(2 * b + 1, 1, weights0, adapter, 0)
                next_weights(2 * b + 1, 1, weights0, adapter, 1)
                adapter = adapter_of(ids1, b + 1, A1)
                sp.wait_ge(rows_turned, PAIRS * (2 * b + 3))
                relay(2 * b + 1, 0, 0)
                relay(2 * b + 1, 1, 0)
                load_x(b + 2, 1, x_landed, x_blocks_landed)
                next_weights(2 * b + 2, 0, weights1, adapter, 0)
                store(b, 2 * b + 2, 0)
                next_weights(2 * b + 2, 0, weights1, adapter, 1)
                store(b, 2 * b + 2, 1)
            adapter = adapter_of(ids1, B - 1, A1)
            next_weights(LAST - 2, 1, weights1, adapter, 0)
            next_weights(LAST - 2, 1, weights1, adapter, 1)
            relay(LAST - 2, 0, 1)
            relay(LAST - 2, 1, 1)
            for h in range(HALVES):
                store(B - 2, LAST - 1, h)
            store(B - 1, LAST, 0)
            for i in range(ROWS):
                store(B - 1, LAST, 1, slice(i, i + 1))
            sp.wait_ge(stored[0], 16 * B)
            sp.wait_ge(stored[1], 16 * (B - 1 + ROWS))

        @block.vector
        def _(dve):
            def turn_weights(stage, parity, u):
                h, pair = u // PAIRS, u % PAIRS
                if isinstance(stage, int) and stage == 0:
                    if u == 0:
                        dve.wait_ge(start_landed, IN_BLOCKS)
                    if u in (PAIRS // 2, PAIRS):
                        dve.wait_ge(raw_landed[0][h], IN_BLOCKS)
                elif pair == 0:
                    dve.wait_ge(raw_landed[parity][h], (stage + 2 - parity) * (IN_BLOCKS // 2))
                if not (isinstance(stage, int) and stage == 0 and u < RING):
                    dve.wait_ge(w_lo_ready, UNITS * stage + u + 1 - RING)
                nc.vector.transpose(
                    turned[:, u % RING, :, :].rearrange("p t (b k) -> p t b k", k=BLOCK),
                    raw[parity][h][:, :, 2 * BLOCK * pair:2 * BLOCK * (pair + 1)]
                    .rearrange("p b (t r) -> p t b r", t=2),
                ).then_inc(w_turned, 1)

            def turn_rows(parity, g):
                nc.vector.transpose(
                    a_turned[g][:, :, :].rearrange("p t (c k) -> p t c k", k=BLOCK),
                    blocks[parity][:, :, 2 * BLOCK * g:2 * BLOCK * (g + 1)].rearrange("p c (t r) -> p t c r", t=2),
                ).then_inc(rows_turned, 1)

            def row_remainders(stage, parity, g):
                dve.wait_ge(a_hi_ready, PAIRS * stage + g + 1)
                nc.vector.tensor_tensor(a_lo[parity][:, 2 * g:2 * g + 2, :], a_turned[g][:, :, :],
                                        a_hi[parity][:, 2 * g:2 * g + 2, :].bitcast(F32),
                                        ALU.subtract).then_inc(a_lo_ready, 1)

            def add_rows(parity, h, i, result):
                cols = slice(BANK * h, BANK * (h + 1))
                nc.vector.tensor_tensor(result[:, i, cols], acc[h][i][:, :], kept[parity][:, i, cols],
                                        ALU.add).then_inc(added, 1)

            def add_half(stage, parity, h, kept_landed, result, batch):
                dve.wait_ge(multiplied, UNITS * stage + PAIRS * (h + 1))
                if h == 0:
                    dve.wait_ge(*kept_landed)
                if result is out_rows:
                    if not (isinstance(batch, int) and batch == 0):
                        dve.wait_ge(stored[h], 16 * batch)
                elif h == 0 and not (isinstance(batch, int) and batch == 0):
                    dve.wait_ge(relaid, RELAID * batch)
                    dve.wait_ge(mid_kept, ROWS * batch)
                for i in range(ROWS):
                    add_rows(parity, h, i, result)

            def run_stage(stage, parity, mine, before, next_blocks):
                for u in range(UNITS):
                    if u + LEAD < UNITS:
                        turn_weights(stage, parity, u + LEAD)
                    elif next_blocks:
                        turn_weights(stage + 1, 1 - parity, u + LEAD - UNITS)
                    if u == 0 and before:
                        add_half(stage - 1, 1 - parity, 1, *before)
                        row_remainders(stage, parity, PAIRS - 1)
                    if u == PAIRS:
                        add_half(stage, parity, 0, *mine)
                    if u >= ROWS_AT and next_blocks:
                        if u == ROWS_AT:
                            dve.wait_ge(*next_blocks)
                        turn_rows(1 - parity, u - ROWS_AT)
                        if u > ROWS_AT:
                            row_remainders(stage + 1, 1 - parity, u - ROWS_AT - 1)

            def l0(b, landed=x_landed):
                return (landed, 16 if landed is x0_landed else 16 * b), mid_rows, b

            def l1(b):
                return (mid_kept, ROWS * (b + 1)), out_rows, b

            dve.wait_ge(x0_blocks_landed, IN_BLOCKS)
            turn_rows(0, 0)
            for g in range(1, PAIRS):
                turn_rows(0, g)
                row_remainders(0, 0, g - 1)
            row_remainders(0, 0, PAIRS - 1)
            for u in range(LEAD):
                turn_weights(0, 0, u)
            run_stage(0, 0, l0(0, x0_landed), None, (x_blocks_landed, IN_BLOCKS))
            run_stage(1, 1, l0(1), l0(0, x0_landed), (relaid, RELAID))
            run_stage(2, 0, l1(0), l0(1), (x_blocks_landed, IN_BLOCKS * 2))
            run_stage(3, 1, l0(2), l1(0), (relaid, RELAID * 2))
            with dve.Fori(1, B - 2) as b:
                run_stage(2 * b + 2, 0, l1(b), l0(b + 1), (x_blocks_landed, IN_BLOCKS * (b + 2)))
                run_stage(2 * b + 3, 1, l0(b + 2), l1(b), (relaid, RELAID * (b + 2)))
            run_stage(LAST - 1, 0, l1(B - 2), l0(B - 1), (relaid, RELAID * B))
            run_stage(LAST, 1, l1(B - 1), l1(B - 2), None)
            dve.wait_ge(stored[1], 16 * (B - 1))
            dve.wait_ge(first_rows_closed, 1)
            add_rows(1, 1, 0, out_rows)
            dve.wait_ge(multiplied, UNITS * (LAST + 1))
            add_rows(1, 1, 1, out_rows)

        @block.scalar
        def _(act):
            def round_weights(stage, u):
                if not (isinstance(stage, int) and stage == 0 and u < RING):
                    act.wait_ge(multiplied, UNITS * stage + u + 1 - RING)
                act.wait_ge(w_turned, UNITS * stage + u + 1)
                nc.scalar.copy(w_hi[:, u % RING, :, :], turned[:, u % RING, :, :]).then_inc(w_hi_ready, 1)

            def round_rows(stage, parity, g):
                act.wait_ge(rows_turned, PAIRS * stage + g + 1)
                nc.scalar.copy(a_hi[parity][:, 2 * g:2 * g + 2, :], a_turned[g][:, :, :]).then_inc(a_hi_ready, 1)

            def run_stage(stage, parity, keeps, last=False):
                for u in range(UNITS):
                    if u + LEAD < UNITS:
                        round_weights(stage, u + LEAD)
                    elif not last:
                        round_weights(stage + 1, u + LEAD - UNITS)
                    if u < ROWS and keeps:
                        if u == 0:
                            act.wait_ge(added, ADDS * stage)
                        nc.scalar.copy(kept[1 - parity][:, u, :], mid_rows[:, u, :]).then_inc(mid_kept, 1)
                    if u >= ROWS_AT and not last:
                        round_rows(stage + 1, 1 - parity, u - ROWS_AT)

            for q in range(QUADRANTS):
                act.dma_start(blocks[0][BLOCK * q:BLOCK * (q + 1), :, :],
                              x[0, :, WIDE * q:WIDE * (q + 1)].rearrange("(c r) j -> r c j", r=BLOCK)
                              ).then_inc(x0_blocks_landed, 16)
            act.dma_start(kept[0][:, :, :], x[0].rearrange("(i p) j -> p i j", p=P)).then_inc(x0_landed, 16)
            for g in range(PAIRS):
                round_rows(0, 0, g)
            for u in range(LEAD):
                round_weights(0, u)
            run_stage(0, 0, keeps=False)
            with act.Fori(0, B - 2) as b:
                run_stage(2 * b + 1, 1, keeps=True)
                run_stage(2 * b + 2, 0, keeps=False)
            run_stage(LAST - 2, 1, keeps=True)
            run_stage(LAST - 1, 0, keeps=True)
            run_stage(LAST, 1, keeps=False, last=True)

        @block.gpsimd
        def _(pool):
            with pool.Fori(0, (LAST + 1) * UNITS // RING) as turn_of_ring:
                for slot in range(RING):
                    pool.wait_ge(w_hi_ready, RING * turn_of_ring + slot + 1)
                    nc.gpsimd.tensor_tensor(w_lo[:, slot, :, :], turned[:, slot, :, :],
                                            w_hi[:, slot, :, :].bitcast(F32), ALU.subtract).then_inc(w_lo_ready, 1)

        @block.tensor
        def _(pe):
            def run_stage(stage, parity, last=False):
                for u in range(UNITS):
                    h, pair = u // PAIRS, u % PAIRS
                    if h == 0:
                        pe.wait_ge(a_lo_ready, PAIRS * stage + pair + 1)
                    if pair == 0 and not (isinstance(stage, int) and stage == 0):
                        pe.wait_ge(added, ADDS * (stage - 1) + ROWS * (h + 1))
                    pe.wait_ge(w_lo_ready, UNITS * stage + u + 1)
                    for i in range(ROWS):
                        mine = slice(P * i, P * (i + 1))
                        for t in range(2):
                            tile = 2 * pair + t
                            hi, lo = a_hi[parity][:, tile, mine], a_lo[parity][:, tile, mine]
                            done = None
                            for rows, weights in ((hi, w_hi), (hi, w_lo), (lo, w_hi)):
                                done = pe.matmul(acc[h][i][:, :], rows, weights[:, u % RING, t, :],
                                                 start=tile == 0 and rows is hi and weights is w_hi,
                                                 stop=tile == TILES - 1 and rows is lo)
                        if last and u == UNITS - 1 and i == 0:
                            done.then_inc(first_rows_closed, 1)
                    done.then_inc(multiplied, 1)

            run_stage(0, 0)
            with pe.Fori(0, B - 1) as b:
                run_stage(2 * b + 1, 1)
                run_stage(2 * b + 2, 0)
            run_stage(LAST, 1, last=True)


def kernel(x, itok_B_1_14, itok_B_3_7, L0_cond_weight, L1_cond_weight):
    import numpy as np
    import concourse.bacc as bacc
    from concourse.bass_utils import run_bass_kernel_spmd

    nc = bacc.Bacc("TRN2", target_bir_lowering=False, num_devices=1)
    arrays = {
        "x": np.ascontiguousarray(x),
        "ids0": np.ascontiguousarray(itok_B_1_14).reshape(1, -1),
        "ids1": np.ascontiguousarray(itok_B_3_7).reshape(1, -1),
        "weights0": np.ascontiguousarray(L0_cond_weight),
        "weights1": np.ascontiguousarray(L1_cond_weight),
    }
    ins = [nc.dram_tensor(n, a.shape, mybir.dt.from_np(a.dtype), kind="ExternalInput").ap()
           for n, a in arrays.items()]
    out = nc.dram_tensor("out", arrays["x"].shape, F32, kind="ExternalOutput").ap()
    residual_adapters(nc, *ins, out)
    return run_bass_kernel_spmd(nc, [arrays], core_ids=[0]).results[0]["out"]
```

```python
from contextlib import ExitStack

import concourse.bass as bass
from concourse import mybir
from concourse.alu_op_type import AluOpType as ALU

F32 = mybir.dt.float32
F32R = mybir.dt.float32r
P = 128
QUADRANTS = 4
BLOCK = P // QUADRANTS
BANK = 512
RING = 4
LEAD = 3
WARM_UP = 34
ROWS_AT = 4


def residual_adapters(nc, x, ids0, ids1, weights0, weights1, out):
    B, S, D = x.shape
    A0, A1 = weights0.shape[0], weights1.shape[0]
    ROWS = S // P
    TILES = D // P
    HALVES = D // BANK
    PAIRS = TILES // 2
    UNITS = HALVES * PAIRS
    WIDE = D // QUADRANTS
    LAST = 2 * B - 1
    ADDS = HALVES * ROWS
    IN_BLOCKS = 16 * QUADRANTS
    RELAID = 16 * QUADRANTS * QUADRANTS
    assert ROWS == 2 and HALVES == 2 and PAIRS == RING and TILES * BLOCK == WIDE and ROWS_AT + PAIRS == UNITS

    with ExitStack() as ctx:
        def sb(name, shape, dtype):
            return ctx.enter_context(nc.sbuf_tensor(name, shape, dtype))

        def sem(name):
            return ctx.enter_context(nc.semaphore(name))

        raw = [[sb(f"raw{s}{h}", [P, BANK // BLOCK, WIDE], F32) for h in range(HALVES)] for s in range(2)]
        blocks = [sb(f"blocks{s}", [P, S // BLOCK, WIDE], F32) for s in range(2)]
        kept = [sb(f"kept{s}", [P, ROWS, D], F32) for s in range(2)]
        a_hi = [sb(f"a_hi{s}", [P, TILES, S], F32R) for s in range(2)]
        a_lo = [sb(f"a_lo{s}", [P, TILES, S], F32R) for s in range(2)]
        turned = sb("turned", [P, RING, 2, BANK], F32)
        w_hi = sb("w_hi", [P, RING, 2, BANK], F32R)
        w_lo = sb("w_lo", [P, RING, 2, BANK], F32R)
        warm = sb("warm", [P, BANK], mybir.dt.bfloat16)
        mid_rows = sb("mid_rows", [P, ROWS, D], F32)
        out_rows = sb("out_rows", [P, ROWS, D], F32)
        acc = [[ctx.enter_context(nc.psum_tensor(f"acc{h}{i}", [P, BANK], F32)) for i in range(ROWS)]
               for h in range(HALVES)]
        a_turned = [ctx.enter_context(nc.psum_tensor(f"a_turned{g}", [P, 2, S], F32)) for g in range(PAIRS)]

        raw_landed = [[sem(f"raw_landed{s}{h}") for h in range(HALVES)] for s in range(2)]
        start_landed = [[sem(f"start_landed{h}{part}") for part in range(2)] for h in range(HALVES)]
        stage1_landed = sem("stage1_landed")
        x0_blocks_landed = [sem(f"x0_blocks_landed{part}") for part in range(2)]
        x_blocks_landed = sem("x_blocks_landed")
        x0_landed = sem("x0_landed")
        x_landed = sem("x_landed")
        warm_ready = sem("warm_ready")
        relaid = sem("relaid")
        mid_kept = sem("mid_kept")
        w_turned = sem("w_turned")
        w_hi_ready = sem("w_hi_ready")
        w_lo_ready = sem("w_lo_ready")
        rows_turned = sem("rows_turned")
        a_hi_ready = sem("a_hi_ready")
        a_lo_ready = sem("a_lo_ready")
        multiplied = sem("multiplied")
        first_rows_closed = sem("first_rows_closed")
        added = sem("added")
        stored = [sem(f"stored{h}") for h in range(HALVES)]

        def load_first_x(queue, part):
            for q in range(QUADRANTS):
                cols = slice(part * (WIDE // 2), (part + 1) * (WIDE // 2))
                queue.dma_start(blocks[0][BLOCK * q:BLOCK * (q + 1), :, cols],
                                x[0, :, WIDE * q:WIDE * (q + 1)].rearrange("(c r) j -> r c j", r=BLOCK)[:, :, cols]
                                ).then_inc(x0_blocks_landed[part], 16)

        block = ctx.enter_context(nc.Block())

        @block.sync
        def _(sp):
            def load_weights(weights, adapter, parity, h, first=0, last=WIDE, landed=None):
                for q in range(QUADRANTS):
                    sp.dma_start(
                        raw[parity][h][BLOCK * q:BLOCK * (q + 1), :, first:last],
                        weights[adapter, BANK * h:BANK * (h + 1), WIDE * q + first:WIDE * q + last]
                        .rearrange("(b k) j -> k b j", k=BLOCK),
                    ).then_inc(landed or raw_landed[parity][h], 16)

            def adapter_of(ids, b, count):
                return sp.value_load(ids[0:1, bass.ds(b, 1)], min_val=0, max_val=count - 1)

            def next_weights(stage, parity, weights, adapter, h):
                sp.wait_ge(w_turned, UNITS * stage + PAIRS * (h + 1))
                load_weights(weights, adapter, parity, h)

            def load_x_blocks(b):
                for q in range(QUADRANTS):
                    sp.dma_start(blocks[1][BLOCK * q:BLOCK * (q + 1), :, :],
                                 x[b, :, WIDE * q:WIDE * (q + 1)].rearrange("(c r) j -> r c j", r=BLOCK)
                                 ).then_inc(x_blocks_landed, 16)

            def load_x_kept(b, parity, landed):
                sp.dma_start(kept[parity][:, :, :], x[b].rearrange("(i p) j -> p i j", p=P)).then_inc(landed, 16)

            def relay(stage, h, parity):
                sp.wait_ge(added, ADDS * stage + ROWS * (h + 1))
                for q in range(QUADRANTS // HALVES * h, QUADRANTS // HALVES * (h + 1)):
                    for g in range(QUADRANTS):
                        sp.dma_start(blocks[parity][BLOCK * q:BLOCK * (q + 1), g:S // BLOCK:QUADRANTS, :],
                                     mid_rows[BLOCK * g:BLOCK * (g + 1), :, WIDE * q:WIDE * (q + 1)]
                                     ).then_inc(relaid, 16)

            def store(b, stage, h, tiles=slice(0, ROWS)):
                sp.wait_ge(added, ADDS * stage + ROWS * h + tiles.stop)
                cols = slice(BANK * h, BANK * (h + 1))
                sp.dma_start(out[b, :, cols].rearrange("(i p) k -> p i k", p=P)[:, tiles],
                             out_rows[:, tiles, cols]).then_inc(stored[h], 16)

            adapter = adapter_of(ids0, 0, A0)
            load_weights(weights0, adapter, 0, 0, 0, WIDE // 2, start_landed[0][0])
            load_first_x(sp, 1)
            load_weights(weights0, adapter, 0, 0, WIDE // 2, WIDE, start_landed[0][1])
            load_weights(weights0, adapter, 0, 1, 0, WIDE // 2, start_landed[1][0])
            load_weights(weights0, adapter, 0, 1, WIDE // 2, WIDE, start_landed[1][1])
            load_x_kept(0, 0, x0_landed)
            load_x_blocks(1)
            adapter = adapter_of(ids0, 1, A0)
            load_weights(weights0, adapter, 1, 0, 0, WIDE // 2, stage1_landed)
            load_weights(weights0, adapter, 1, 0, WIDE // 2, WIDE)
            load_x_kept(1, 1, x_landed)
            load_weights(weights0, adapter, 1, 1)
            adapter = adapter_of(ids1, 0, A1)
            next_weights(0, 0, weights1, adapter, 0)
            relay(0, 0, 0)
            relay(0, 1, 0)
            next_weights(0, 0, weights1, adapter, 1)
            with sp.Fori(0, B - 2) as b:
                sp.wait_ge(rows_turned, PAIRS * (2 * b + 2))
                load_x_blocks(b + 2)
                adapter = adapter_of(ids0, b + 2, A0)
                next_weights(2 * b + 1, 1, weights0, adapter, 0)
                next_weights(2 * b + 1, 1, weights0, adapter, 1)
                adapter = adapter_of(ids1, b + 1, A1)
                sp.wait_ge(rows_turned, PAIRS * (2 * b + 3))
                relay(2 * b + 1, 0, 0)
                relay(2 * b + 1, 1, 0)
                load_x_kept(b + 2, 1, x_landed)
                next_weights(2 * b + 2, 0, weights1, adapter, 0)
                store(b, 2 * b + 2, 0)
                next_weights(2 * b + 2, 0, weights1, adapter, 1)
                store(b, 2 * b + 2, 1)
            adapter = adapter_of(ids1, B - 1, A1)
            next_weights(LAST - 2, 1, weights1, adapter, 0)
            next_weights(LAST - 2, 1, weights1, adapter, 1)
            relay(LAST - 2, 0, 1)
            relay(LAST - 2, 1, 1)
            for h in range(HALVES):
                store(B - 2, LAST - 1, h)
            store(B - 1, LAST, 0)
            for i in range(ROWS):
                store(B - 1, LAST, 1, slice(i, i + 1))
            sp.wait_ge(stored[0], 16 * B)
            sp.wait_ge(stored[1], 16 * (B - 1 + ROWS))

        @block.vector
        def _(dve):
            def turn_weights(stage, parity, u):
                h, pair = u // PAIRS, u % PAIRS
                if isinstance(stage, int) and stage == 0:
                    if pair % 2 == 0:
                        dve.wait_ge(start_landed[h][pair // 2], IN_BLOCKS)
                elif isinstance(stage, int) and stage == 1 and u == 0:
                    dve.wait_ge(stage1_landed, IN_BLOCKS)
                elif pair == 0 or isinstance(stage, int) and stage == 1 and u == PAIRS // 2:
                    dve.wait_ge(raw_landed[parity][h], (stage + parity) * (IN_BLOCKS // 2))
                if not (isinstance(stage, int) and stage == 0 and u < RING):
                    dve.wait_ge(w_lo_ready, UNITS * stage + u + 1 - RING)
                nc.vector.transpose(
                    turned[:, u % RING, :, :].rearrange("p t (b k) -> p t b k", k=BLOCK),
                    raw[parity][h][:, :, 2 * BLOCK * pair:2 * BLOCK * (pair + 1)]
                    .rearrange("p b (t r) -> p t b r", t=2),
                ).then_inc(w_turned, 1)

            def turn_rows(parity, g):
                nc.vector.transpose(
                    a_turned[g][:, :, :].rearrange("p t (c k) -> p t c k", k=BLOCK),
                    blocks[parity][:, :, 2 * BLOCK * g:2 * BLOCK * (g + 1)].rearrange("p c (t r) -> p t c r", t=2),
                ).then_inc(rows_turned, 1)

            def row_remainders(stage, parity, g):
                dve.wait_ge(a_hi_ready, PAIRS * stage + g + 1)
                nc.vector.tensor_tensor(a_lo[parity][:, 2 * g:2 * g + 2, :], a_turned[g][:, :, :],
                                        a_hi[parity][:, 2 * g:2 * g + 2, :].bitcast(F32),
                                        ALU.subtract).then_inc(a_lo_ready, 1)

            def add_rows(parity, h, i, result):
                cols = slice(BANK * h, BANK * (h + 1))
                nc.vector.tensor_tensor(result[:, i, cols], acc[h][i][:, :], kept[parity][:, i, cols],
                                        ALU.add).then_inc(added, 1)

            def add_half(stage, parity, h, kept_landed, result, batch):
                dve.wait_ge(multiplied, UNITS * stage + PAIRS * (h + 1))
                if h == 0:
                    dve.wait_ge(*kept_landed)
                if result is out_rows:
                    if not (isinstance(batch, int) and batch == 0):
                        dve.wait_ge(stored[h], 16 * batch)
                elif h == 0 and not (isinstance(batch, int) and batch == 0):
                    dve.wait_ge(relaid, RELAID * batch)
                    dve.wait_ge(mid_kept, ROWS * batch)
                for i in range(ROWS):
                    add_rows(parity, h, i, result)

            def run_stage(stage, parity, mine, before, next_blocks):
                for u in range(UNITS):
                    if u + LEAD < UNITS:
                        turn_weights(stage, parity, u + LEAD)
                    elif next_blocks:
                        turn_weights(stage + 1, 1 - parity, u + LEAD - UNITS)
                    if u == 0 and before:
                        add_half(stage - 1, 1 - parity, 1, *before)
                        row_remainders(stage, parity, PAIRS - 1)
                    if u == PAIRS:
                        add_half(stage, parity, 0, *mine)
                    if u >= ROWS_AT and next_blocks:
                        if u == ROWS_AT:
                            dve.wait_ge(*next_blocks)
                        turn_rows(1 - parity, u - ROWS_AT)
                        if u > ROWS_AT:
                            row_remainders(stage + 1, 1 - parity, u - ROWS_AT - 1)

            def l0(b, landed=x_landed):
                return (landed, 16 if landed is x0_landed else 16 * b), mid_rows, b

            def l1(b):
                return (mid_kept, ROWS * (b + 1)), out_rows, b

            for part in range(2):
                first, second = 2 * part, 2 * part + 1
                dve.wait_ge(x0_blocks_landed[part], IN_BLOCKS)
                turn_rows(0, first)
                turn_rows(0, second)
                row_remainders(0, 0, first)
                row_remainders(0, 0, second)
                turn_weights(0, 0, first)
                if part == 0:
                    turn_weights(0, 0, second)
            run_stage(0, 0, l0(0, x0_landed), None, (x_blocks_landed, IN_BLOCKS))
            run_stage(1, 1, l0(1), l0(0, x0_landed), (relaid, RELAID))
            run_stage(2, 0, l1(0), l0(1), (x_blocks_landed, IN_BLOCKS * 2))
            run_stage(3, 1, l0(2), l1(0), (relaid, RELAID * 2))
            with dve.Fori(1, B - 2) as b:
                run_stage(2 * b + 2, 0, l1(b), l0(b + 1), (x_blocks_landed, IN_BLOCKS * (b + 2)))
                run_stage(2 * b + 3, 1, l0(b + 2), l1(b), (relaid, RELAID * (b + 2)))
            run_stage(LAST - 1, 0, l1(B - 2), l0(B - 1), (relaid, RELAID * B))
            run_stage(LAST, 1, l1(B - 1), l1(B - 2), None)
            dve.wait_ge(stored[1], 16 * (B - 1))
            dve.wait_ge(first_rows_closed, 1)
            add_rows(1, 1, 0, out_rows)
            dve.wait_ge(multiplied, UNITS * (LAST + 1))
            add_rows(1, 1, 1, out_rows)

        @block.scalar
        def _(act):
            def round_weights(stage, u):
                if not (isinstance(stage, int) and stage == 0 and u < RING):
                    act.wait_ge(multiplied, UNITS * stage + u + 1 - RING)
                act.wait_ge(w_turned, UNITS * stage + u + 1)
                nc.scalar.copy(w_hi[:, u % RING, :, :], turned[:, u % RING, :, :]).then_inc(w_hi_ready, 1)

            def round_rows(stage, parity, g):
                act.wait_ge(rows_turned, PAIRS * stage + g + 1)
                nc.scalar.copy(a_hi[parity][:, 2 * g:2 * g + 2, :], a_turned[g][:, :, :]).then_inc(a_hi_ready, 1)

            def run_stage(stage, parity, keeps, last=False):
                for u in range(UNITS):
                    if u + LEAD < UNITS:
                        round_weights(stage, u + LEAD)
                    elif not last:
                        round_weights(stage + 1, u + LEAD - UNITS)
                    if u < ROWS and keeps:
                        if u == 0:
                            act.wait_ge(added, ADDS * stage)
                        nc.scalar.copy(kept[1 - parity][:, u, :], mid_rows[:, u, :]).then_inc(mid_kept, 1)
                    if u >= ROWS_AT and not last:
                        round_rows(stage + 1, 1 - parity, u - ROWS_AT)

            load_first_x(act, 0)
            for g in (0, 1):
                round_rows(0, 0, g)
            for u in (0, 1):
                round_weights(0, u)
            for g in (2, 3):
                round_rows(0, 0, g)
            round_weights(0, 2)
            run_stage(0, 0, keeps=False)
            with act.Fori(0, B - 2) as b:
                run_stage(2 * b + 1, 1, keeps=True)
                run_stage(2 * b + 2, 0, keeps=False)
            run_stage(LAST - 2, 1, keeps=True)
            run_stage(LAST - 1, 0, keeps=True)
            run_stage(LAST, 1, keeps=False, last=True)

        @block.gpsimd
        def _(pool):
            nc.gpsimd.memset(warm[:, :], 0.0).then_inc(warm_ready, 1)
            with pool.Fori(0, (LAST + 1) * UNITS // RING) as turn_of_ring:
                for slot in range(RING):
                    pool.wait_ge(w_hi_ready, RING * turn_of_ring + slot + 1)
                    nc.gpsimd.tensor_tensor(w_lo[:, slot, :, :], turned[:, slot, :, :],
                                            w_hi[:, slot, :, :].bitcast(F32), ALU.subtract).then_inc(w_lo_ready, 1)

        @block.tensor
        def _(pe):
            def run_stage(stage, parity, last=False):
                for u in range(UNITS):
                    h, pair = u // PAIRS, u % PAIRS
                    if h == 0:
                        pe.wait_ge(a_lo_ready, PAIRS * stage + pair + 1)
                    if pair == 0 and not (isinstance(stage, int) and stage == 0):
                        pe.wait_ge(added, ADDS * (stage - 1) + ROWS * (h + 1))
                    pe.wait_ge(w_lo_ready, UNITS * stage + u + 1)
                    for i in range(ROWS):
                        mine = slice(P * i, P * (i + 1))
                        for t in range(2):
                            tile = 2 * pair + t
                            hi, lo = a_hi[parity][:, tile, mine], a_lo[parity][:, tile, mine]
                            for rows, weights in ((hi, w_hi), (hi, w_lo), (lo, w_hi)):
                                done = pe.matmul(acc[h][i][:, :], rows, weights[:, u % RING, t, :],
                                                 start=tile == 0 and rows is hi and weights is w_hi,
                                                 stop=tile == TILES - 1 and rows is lo)
                        if last and u == UNITS - 1 and i == 0:
                            done.then_inc(first_rows_closed, 1)
                    done.then_inc(multiplied, 1)

            pe.wait_ge(warm_ready, 1)
            for _ in range(WARM_UP):
                pe.matmul(acc[0][0][:, :], warm[:, 0:P], warm[:, :], start=True, stop=True)
            run_stage(0, 0)
            with pe.Fori(0, B - 1) as b:
                run_stage(2 * b + 1, 1)
                run_stage(2 * b + 2, 0)
            run_stage(LAST, 1, last=True)


def kernel(x, itok_B_1_14, itok_B_3_7, L0_cond_weight, L1_cond_weight):
    import numpy as np
    import concourse.bacc as bacc
    from concourse.bass_utils import run_bass_kernel_spmd

    nc = bacc.Bacc("TRN2", target_bir_lowering=False, num_devices=1)
    arrays = {
        "x": np.ascontiguousarray(x),
        "ids0": np.ascontiguousarray(itok_B_1_14).reshape(1, -1),
        "ids1": np.ascontiguousarray(itok_B_3_7).reshape(1, -1),
        "weights0": np.ascontiguousarray(L0_cond_weight),
        "weights1": np.ascontiguousarray(L1_cond_weight),
    }
    ins = [nc.dram_tensor(n, a.shape, mybir.dt.from_np(a.dtype), kind="ExternalInput").ap()
           for n, a in arrays.items()]
    out = nc.dram_tensor("out", arrays["x"].shape, F32, kind="ExternalOutput").ap()
    residual_adapters(nc, *ins, out)
    return run_bass_kernel_spmd(nc, [arrays], core_ids=[0]).results[0]["out"]
```
